# Optimizing a Trainium2 kernel written in Bass

```python
import numpy as np
import jax
import jax.numpy as jnp

def _softmax(x, axis=-1):
    return jax.nn.softmax(x, axis=axis)

def _gelu(x):
    return jax.nn.gelu(x, approximate=True)

def _silu(x):
    return jax.nn.silu(x)

def _sigmoid(x):
    return jax.nn.sigmoid(x)

def _layernorm(x, axis=-1, eps=1e-05):
    m = jnp.mean(x, axis=axis, keepdims=True)
    v = jnp.var(x, axis=axis, keepdims=True)
    return (x - m) / jnp.sqrt(v + eps)

def _scatter_add(tgt, idx, src, axis=0):
    return tgt.at[idx].add(src)

def _segment_sum(src, seg, n):
    return jax.ops.segment_sum(src, seg, n)
kernel_name = 'mk_cond_resid_d4_seqx_r4_97d714'

def setup_inputs(seed: int=0):
    np.random.seed(seed)
    _w = jnp.asarray

    def _rec_inputs():
        import jax
        import jax.numpy as jnp
        _rk = jax.random.key(seed)
        x = 7.22e-05 + 1 * jax.random.normal(jax.random.fold_in(_rk, 1), (2, 1024, 256), jnp.float32)
        _lenS = 1024 - jax.random.randint(jax.random.fold_in(_rk, 7), (2,), 0, max(1, 1024 // 4) + 1, jnp.int32)
        _lenS2 = 1024 - jax.random.randint(jax.random.fold_in(_rk, 8), (2,), 0, max(1, 1024 // 4) + 1, jnp.int32)
        cond_8 = -0.104238 + 1.01173 * jax.random.normal(jax.random.fold_in(_rk, 11), (2, 8), jnp.float32)
        return (x, cond_8)
    x, cond_8 = _rec_inputs()

    def _L0_cond_setup():
        import jax, jax.numpy as jnp
        import numpy as np
        TOP_K = 2
        NUM_MOE_LAYERS = 12

        def _gemma_mlp(x, gate_w, up_w, down_w):
            g = jnp.einsum('bsh,hi->bsi', x, gate_w)
            u = jnp.einsum('bsh,hi->bsi', x, up_w)
            return jnp.einsum('bsi,ih->bsh', jax.nn.gelu(g, approximate=True) * u, down_w)
        key = jax.random.key(seed)
        ks = jax.random.split(key, 8)
        B, S, H, I, E = (32, 64, 256, 1024, 8)
        std = 0.02
        return {'x': jax.random.normal(ks[0], (B, S, H), jnp.float32), 'router_logits': jax.random.normal(ks[1], (B, E), jnp.float32), 'skill_gate': jax.random.normal(ks[2], (E, H, I), jnp.float32) * std, 'skill_up': jax.random.normal(ks[3], (E, H, I), jnp.float32) * std, 'skill_down': jax.random.normal(ks[4], (E, I, H), jnp.float32) * std, 'shared_gate': jax.random.normal(ks[5], (H, I), jnp.float32) * std, 'shared_up': jax.random.normal(ks[6], (H, I), jnp.float32) * std, 'shared_down': jax.random.normal(ks[7], (I, H), jnp.float32) * std}
    _L0_cond_all = _L0_cond_setup()
    _L0_cond_in = {k: v for k, v in _L0_cond_all.items() if k in ('skill_gate', 'skill_up', 'skill_down', 'shared_gate', 'shared_up', 'shared_down')}
    del _L0_cond_all

    def _L1_cond_setup():
        import jax, jax.numpy as jnp
        import numpy as np
        R = 16
        ALPHA = 32.0
        SCALING = ALPHA / R
        key = jax.random.key(seed)
        ks = jax.random.split(key, 6)
        B, T, C, O, E = (16, 375, 256, 256, 8)
        x = jax.random.normal(ks[0], (B, T, C), dtype=jnp.float32)
        w = jax.random.uniform(ks[1], (B, E), dtype=jnp.float32)
        W_base = jax.random.normal(ks[2], (O, C), dtype=jnp.float32) * 0.02
        b_base = jax.random.normal(ks[3], (O,), dtype=jnp.float32) * 0.02
        As = jax.random.normal(ks[4], (E, R, C), dtype=jnp.float32) * 0.02
        Bs = jax.random.normal(ks[5], (E, O, R), dtype=jnp.float32) * 0.02
        return {'x': x, 'w': w, 'W_base': W_base, 'b_base': b_base, 'As': As, 'Bs': Bs}
    _L1_cond_all = _L1_cond_setup()
    _L1_cond_in = {k: v for k, v in _L1_cond_all.items() if k in ('W_base', 'b_base', 'As', 'Bs')}
    del _L1_cond_all

    def _L2_cond_setup():
        import jax, jax.numpy as jnp
        import numpy as np
        key = jax.random.key(seed)
        k1, k2, k3, k4, k5 = jax.random.split(key, 5)
        B, N, T, O, G = (32, 64, 256, 256, 8)
        x = jax.random.normal(k1, (B, N, T), dtype=jnp.float32)
        y = jax.random.uniform(k2, (B, G), dtype=jnp.float32)
        weight = jax.random.normal(k3, (G, O, T), dtype=jnp.float32) * (1.0 / np.sqrt(T))
        mask = jax.random.uniform(k4, (O, T), dtype=jnp.float32)
        bias = jax.random.normal(k5, (O,), dtype=jnp.float32)
        return {'x': x, 'y': y, 'weight': weight, 'mask': mask, 'bias': bias}
    _L2_cond_all = _L2_cond_setup()
    _L2_cond_in = {k: v for k, v in _L2_cond_all.items() if k in ('weight', 'mask', 'bias')}
    del _L2_cond_all

    def _L3_cond_setup():
        import jax, jax.numpy as jnp
        import numpy as np
        key = jax.random.key(seed)
        k1, k2, k3, k4, k5 = jax.random.split(key, 5)
        B, N, T, O, G = (32, 64, 256, 256, 8)
        x = jax.random.normal(k1, (B, N, T), dtype=jnp.float32)
        y = jax.random.uniform(k2, (B, G), dtype=jnp.float32)
        weight = jax.random.normal(k3, (G, O, T), dtype=jnp.float32) * (1.0 / np.sqrt(T))
        mask = jax.random.uniform(k4, (O, T), dtype=jnp.float32)
        bias = jax.random.normal(k5, (O,), dtype=jnp.float32)
        return {'x': x, 'y': y, 'weight': weight, 'mask': mask, 'bias': bias}
    _L3_cond_all = _L3_cond_setup()
    _L3_cond_in = {k: v for k, v in _L3_cond_all.items() if k in ('weight', 'mask', 'bias')}
    del _L3_cond_all
    return {'x': x, 'cond_8': cond_8, 'L0_cond_skill_gate': _L0_cond_in['skill_gate'], 'L0_cond_skill_up': _L0_cond_in['skill_up'], 'L0_cond_skill_down': _L0_cond_in['skill_down'], 'L0_cond_shared_gate': _L0_cond_in['shared_gate'], 'L0_cond_shared_up': _L0_cond_in['shared_up'], 'L0_cond_shared_down': _L0_cond_in['shared_down'], 'L1_cond_W_base': _L1_cond_in['W_base'], 'L1_cond_b_base': _L1_cond_in['b_base'], 'L1_cond_As': _L1_cond_in['As'], 'L1_cond_Bs': _L1_cond_in['Bs'], 'L2_cond_weight': _L2_cond_in['weight'], 'L2_cond_mask': _L2_cond_in['mask'], 'L2_cond_bias': _L2_cond_in['bias'], 'L3_cond_weight': _L3_cond_in['weight'], 'L3_cond_mask': _L3_cond_in['mask'], 'L3_cond_bias': _L3_cond_in['bias']}

def reference(x, cond_8, L0_cond_skill_gate, L0_cond_skill_up, L0_cond_skill_down, L0_cond_shared_gate, L0_cond_shared_up, L0_cond_shared_down, L1_cond_W_base, L1_cond_b_base, L1_cond_As, L1_cond_Bs, L2_cond_weight, L2_cond_mask, L2_cond_bias, L3_cond_weight, L3_cond_mask, L3_cond_bias):
    import jax
    import jax.numpy as jnp

    def _L0_cond_ref(x, router_logits, skill_gate, skill_up, skill_down, shared_gate, shared_up, shared_down):
        import jax, jax.numpy as jnp
        import numpy as np
        TOP_K = 2
        NUM_MOE_LAYERS = 12

        def _gemma_mlp(x, gate_w, up_w, down_w):
            g = jnp.einsum('bsh,hi->bsi', x, gate_w)
            u = jnp.einsum('bsh,hi->bsi', x, up_w)
            return jnp.einsum('bsi,ih->bsh', jax.nn.gelu(g, approximate=True) * u, down_w)
        B = x.shape[0]
        E = skill_gate.shape[0]
        rw = jax.nn.softmax(router_logits.astype(jnp.float32), axis=-1)
        w, sel = jax.lax.top_k(rw, TOP_K)
        w = w / w.sum(axis=-1, keepdims=True)
        w = w.astype(x.dtype)
        scale = 1.0 / NUM_MOE_LAYERS
        w = scale * w + (1.0 - scale) * jax.lax.stop_gradient(w)
        dense_w = jnp.zeros((B, E), x.dtype).at[jnp.arange(B)[:, None], sel].add(w)

        def step(acc, params):
            g, u, d, we = params
            return (acc + we[:, None, None] * _gemma_mlp(x, g, u, d), None)
        out, _ = jax.lax.scan(step, jnp.zeros_like(x), (skill_gate, skill_up, skill_down, dense_w.T))
        out = out + _gemma_mlp(x, shared_gate, shared_up, shared_down)
        return out

    def _L1_cond_ref(x, w, W_base, b_base, As, Bs):
        import jax, jax.numpy as jnp
        import numpy as np
        R = 16
        ALPHA = 32.0
        SCALING = ALPHA / R
        out = jnp.einsum('btc,oc->bto', x, W_base) + b_base
        h = jnp.einsum('btc,erc->bter', x, As)
        lora = jnp.einsum('bter,eor,be->bto', h, Bs, w)
        return out + lora * SCALING

    def _L2_cond_ref(x, y, weight, mask, bias):
        import jax, jax.numpy as jnp
        import numpy as np
        masked_w = weight * mask[None, :, :]
        w_bot = jnp.einsum('bg,got->bot', y, masked_w)
        return jnp.einsum('bnt,bot->bno', x, w_bot) + bias

    def _L3_cond_ref(x, y, weight, mask, bias):
        import jax, jax.numpy as jnp
        import numpy as np
        masked_w = weight * mask[None, :, :]
        w_bot = jnp.einsum('bg,got->bot', y, masked_w)
        return jnp.einsum('bnt,bot->bno', x, w_bot) + bias
    x = x + _L0_cond_ref(x, cond_8, L0_cond_skill_gate, L0_cond_skill_up, L0_cond_skill_down, L0_cond_shared_gate, L0_cond_shared_up, L0_cond_shared_down)
    x = x + _L1_cond_ref(x, cond_8, L1_cond_W_base, L1_cond_b_base, L1_cond_As, L1_cond_Bs)
    x = x + _L2_cond_ref(x, cond_8, L2_cond_weight, L2_cond_mask, L2_cond_bias)
    x = x + _L3_cond_ref(x, cond_8, L3_cond_weight, L3_cond_mask, L3_cond_bias)
    return x

_drawn_inputs = setup_inputs


def setup_inputs(seed=0):
    import zlib

    import numpy as np

    out = dict(_drawn_inputs(seed))
    spreads = {}
    factors = {'L1_cond_b_base': 3.615}
    for name, (base, spread) in spreads.items():
        noise = np.random.default_rng([zlib.crc32(name.encode()), seed]).standard_normal(out[name].shape)
        drawn = base * np.exp(spread * noise) if base else spread * noise
        out[name] = jnp.asarray(drawn.astype(out[name].dtype))
    for name, factor in factors.items():
        out[name] = (out[name] * factor).astype(out[name].dtype)
    return out
```

```python
from contextlib import ExitStack

import concourse.bass as bass
import concourse.mybir as mybir

P = 128
F32 = mybir.dt.float32
F32R = mybir.dt.float32r
U32 = mybir.dt.uint32
ALU = mybir.AluOpType
ACT = mybir.ActivationFunctionType
AX = mybir.AxisListType

BATCHES = 2
TOKENS = 1024
HID = 256
INNER = 1024
EXPERTS = 8
GROUPS = 8
RANK = 16
TOP_K = 2
MOE_LAYERS = 12
LORA_SCALING = 32.0 / RANK

KT = HID // P
TN = 512
HALVES = TOKENS // TN
CPE = INNER // P
SHARED = EXPERTS
JOBS = 1 + TOP_K
CHUNKS = JOBS * CPE
PAIRS = CHUNKS // 2
PPE = CPE // 2
FOLD_PAIR = 8
GU = 2 * KT * P


def bass_moe_lora_masked_mixtures(nc, xT, cond, w_gate_up, w_down, w_base, lora_a, lora_b,
                                  mix2, mask2, mix3, mask3, biases, outT):
    with ExitStack() as ctx:
        def sb(name, shape, dt=F32):
            return ctx.enter_context(nc.sbuf_tensor(name, shape, dt))

        def bank(name):
            return ctx.enter_context(nc.psum_tensor(name, [P, TN], F32))

        def sem(name):
            return ctx.enter_context(nc.semaphore(name))

        x = sb("x", [P, BATCHES, KT, TOKENS])
        x_high = sb("x_high", [P, BATCHES, KT, TOKENS], F32R)
        x_low = sb("x_low", [P, BATCHES, KT, TOKENS], F32R)
        gu_raw = sb("gu_raw", [P, 2, GU])
        gu_high = sb("gu_high", [P, 2, GU], F32R)
        gu_low = sb("gu_low", [P, 2, GU], F32R)
        dn_raw = sb("dn_raw", [P, 2, HID])
        dn_high = sb("dn_high", [P, 2, HID], F32R)
        dn_low = sb("dn_low", [P, 2, HID], F32R)
        gelu = sb("gelu", [P, HALVES, TN])
        hidden = sb("hidden", [P, HALVES, TN])
        h_high = sb("h_high", [P, 2, HALVES, TN], F32R)
        h_low = sb("h_low", [P, 2, HALVES, TN], F32R)
        y = sb("y", [P, KT, TOKENS])
        logits = sb("logits", [P, BATCHES, EXPERTS])
        top = sb("top", [P, BATCHES, EXPERTS])
        pick = sb("pick", [P, BATCHES, EXPERTS], U32)
        pick_safe = sb("pick_safe", [P, BATCHES, EXPERTS], U32)
        neg_max = sb("neg_max", [P, BATCHES])
        prob = sb("prob", [P, BATCHES, EXPERTS])
        prob_sum = sb("prob_sum", [P, BATCHES])
        top_w = sb("top_w", [P, BATCHES, TOP_K])
        top_scaled = sb("top_scaled", [P, BATCHES, TOP_K])
        pair_weight = sb("pair_weight", [P, BATCHES * PAIRS])
        lora_w = sb("lora_w", [P, BATCHES])
        lora_w2 = sb("lora_w2", [P, BATCHES])
        la = sb("la", [P, HID])
        la_w = sb("la_w", [P, BATCHES, HID])
        lb = sb("lb", [P, HID])
        eye = sb("eye", [P, KT, HID])
        base = sb("base", [P, KT, HID])
        m2 = sb("m2", [P, KT, HID])
        m3 = sb("m3", [P, KT, HID])
        g2 = sb("g2", [P, GROUPS, KT * HID])
        g3 = sb("g3", [P, GROUPS, KT * HID])
        term = sb("term", [P, KT * HID])
        bias = sb("bias", [P, 3, KT])
        a1 = sb("a1", [P, BATCHES, KT, HID])
        a2 = sb("a2", [P, BATCHES, KT, HID])
        r3 = sb("r3", [P, BATCHES, KT, HID])
        r23 = sb("r23", [P, BATCHES, KT, HID])
        fold = sb("fold", [P, BATCHES, KT, HID])
        fold_high = sb("fold_high", [P, BATCHES, KT, HID], F32R)
        fold_low = sb("fold_low", [P, BATCHES, KT, HID], F32R)
        bias_out = sb("bias_out", [P, BATCHES, KT])

        gate = [bank(f"gate{i}") for i in range(HALVES)]
        up = [bank(f"up{i}") for i in range(HALVES)]
        acc = [[bank(f"acc{k}_{t}") for t in range(HALVES)] for k in range(KT)]

        cond_in = sem("cond_in")
        lora_w_in = sem("lora_w_in")
        x_in = [[sem(f"x_in{b}_{t}") for t in range(HALVES)] for b in range(BATCHES)]
        gu_in = [sem(f"gu_in{i}") for i in range(2)]
        dn_in = [sem(f"dn_in{i}") for i in range(2)]
        mix2_in = sem("mix2_in")
        mix3_in = sem("mix3_in")
        small_in = sem("small_in")
        top_done = sem("top_done")
        pick_found = sem("pick_found")
        pick_done = sem("pick_done")
        neg_done = sem("neg_done")
        exp_done = sem("exp_done")
        route_step = sem("route_step")
        xh_done = sem("xh_done")
        xl_done = sem("xl_done")
        guh_done = sem("guh_done")
        gul_done = sem("gul_done")
        dnh_done = sem("dnh_done")
        dnl_done = sem("dnl_done")
        gate_done = sem("gate_done")
        up_done = sem("up_done")
        gelu_done = sem("gelu_done")
        h_done = sem("h_done")
        hh_done = sem("hh_done")
        hl_done = sem("hl_done")
        down_done = sem("down_done")
        pool_step = sem("pool_step")
        la_done = sem("la_done")
        base_done = sem("base_done")
        mixes_done = sem("mixes_done")
        fold_mm = sem("fold_mm")
        fold_out = sem("fold_out")
        foldh_done = sem("foldh_done")
        foldl_done = sem("foldl_done")
        x1_done = sem("x1_done")
        x1h_done = sem("x1h_done")
        x1l_done = sem("x1l_done")
        final_mm = sem("final_mm")
        final_out = sem("final_out")
        stored = sem("stored")

        block = ctx.enter_context(nc.Block())

        @block.sync
        def _(sp):
            def load(slot, expert, chunk, turn):
                if turn is not None:
                    sp.wait_ge(guh_done, 2 * turn - 1 + slot)
                    sp.wait_ge(gul_done, 2 * turn - 1 + slot)
                sp.dma_start(gu_raw[:, slot, :], w_gate_up[expert, chunk]).then_inc(gu_in[slot], 16)
                if turn is not None:
                    sp.wait_ge(dnh_done, 2 * turn - 1 + slot)
                    sp.wait_ge(dnl_done, 2 * turn - 1 + slot)
                sp.dma_start(dn_raw[:, slot, :], w_down[expert, chunk]).then_inc(dn_in[slot], 16)

            load(0, SHARED, 0, None)
            load(1, SHARED, 1, None)
            for t in range(HALVES):
                sp.dma_start(x[:, 1, :, t * TN:(t + 1) * TN], xT[1, t]).then_inc(x_in[1][t], 16)
            for dst, src in ((la, lora_a), (lb, lora_b), (base, w_base), (m2, mask2), (m3, mask3), (bias, biases)):
                sp.dma_start(dst[:], src).then_inc(small_in, 16)
            with sp.Fori(1, PPE) as p:
                load(0, SHARED, 2 * p, p)
                load(1, SHARED, 2 * p + 1, p)
            sp.dma_start(g2[:, :, :], mix2).then_inc(mix2_in, 16)
            sp.dma_start(g3[:, :, :], mix3).then_inc(mix3_in, 16)
            sp.wait_ge(pick_done, 1)
            for b in range(BATCHES):
                for j in range(b == 0, JOBS):
                    if j == 0:
                        expert = SHARED
                    else:
                        expert = sp.value_load(pick_safe[0:1, b, j - 1:j], min_val=0, max_val=EXPERTS - 1)
                    first = b * PAIRS + j * PPE
                    with sp.Fori(0, PPE) as p:
                        load(0, expert, 2 * p, p + first)
                        load(1, expert, 2 * p + 1, p + first)

        @block.gpsimd
        def _(pool):
            steps = 0

            def step(ins):
                nonlocal steps
                steps += 1
                ins.then_inc(pool_step, 1)
                pool.wait_ge(pool_step, steps)

            step(pool.memset(eye[:], 0.0))
            for k in range(KT):
                step(pool.affine_select(out=eye[:, k, :], in_=eye[:, k, :], compare_op=ALU.not_equal, fill=1.0,
                                        base=k * P, pattern=[[-1, HID]], channel_multiplier=1))
            pool.wait_ge(cond_in, 16)
            pool.wait_ge(lora_w_in, 16 * BATCHES)
            pool.wait_ge(small_in, 16 * 6)
            step(pool.tensor_scalar(lora_w2[:], lora_w[:], LORA_SCALING, 0.0, ALU.mult, ALU.add))
            for b in range(BATCHES):
                pool.tensor_scalar(la_w[:, b, :], la[:], lora_w2[:, b:b + 1], 0.0, ALU.mult, ALU.add
                                   ).then_inc(la_done, 1)
            pool.tensor_tensor(base[:], base[:], eye[:], ALU.add).then_inc(base_done, 1)
            for mix, mask, out, arrived in ((g2, m2, a2, mix2_in), (g3, m3, r3, mix3_in)):
                pool.wait_ge(arrived, 16)
                for b in range(BATCHES):
                    dst = out[:, b].rearrange("p k n -> p (k n)")
                    step(pool.tensor_scalar(dst, mix[:, 0, :], logits[:, b, 0:1], 0.0, ALU.mult, ALU.add))
                    for g in range(1, GROUPS):
                        step(pool.tensor_scalar(term[:], mix[:, g, :], logits[:, b, g:g + 1], 0.0, ALU.mult, ALU.add))
                        step(pool.tensor_tensor(dst, dst, term[:], ALU.add))
                    step(pool.tensor_tensor(out[:, b], out[:, b], mask[:], ALU.mult))
                    pool.tensor_tensor(out[:, b], out[:, b], eye[:], ALU.add).then_inc(mixes_done, 1)
            for b in range(BATCHES):
                for t in range(HALVES):
                    for k in range(KT):
                        pool.wait_ge(final_out, 1 + k + KT * (t + HALVES * b))
                        pool.dma_start(outT[b, k, :, t * TN:(t + 1) * TN],
                                       y[:, k, t * TN:(t + 1) * TN]).then_inc(stored, 16)
            pool.wait_ge(stored, 16 * BATCHES * HALVES * KT)

        @block.scalar
        def _(act):
            act.dma_start(logits[:].rearrange("p b e -> p (b e)"),
                          cond.rearrange("b e -> (b e)").unsqueeze(0).to_broadcast([P, BATCHES * EXPERTS])
                          ).then_inc(cond_in, 16)
            for t in range(HALVES):
                act.dma_start(x[:, 0, :, t * TN:(t + 1) * TN], xT[0, t]).then_inc(x_in[0][t], 16)
            for b in range(BATCHES):
                act.dma_start(lora_w[:, b:b + 1],
                              cond[b].unsqueeze(1).to_broadcast([EXPERTS, RANK])
                              ).then_inc(lora_w_in, 16)

            def split_x_high(b, t):
                act.wait_ge(x_in[b][t], 16)
                act.copy(x_high[:, b, :, t * TN:(t + 1) * TN],
                         x[:, b, :, t * TN:(t + 1) * TN]).then_inc(xh_done, 1)

            def split_gate_up(slot, c, turn):
                act.wait_ge(gu_in[slot], 16 * turn + 16)
                if not isinstance(c, int) or c >= 2:
                    act.wait_ge(up_done, 2 * c - 2)
                act.copy(gu_high[:, slot, :], gu_raw[:, slot, :]).then_inc(guh_done, 1)

            def split_down(slot, c, turn):
                act.wait_ge(dn_in[slot], 16 * turn + 16)
                if not isinstance(c, int) or c >= 2:
                    act.wait_ge(down_done, 2 * c - 2)
                act.copy(dn_high[:, slot, :], dn_raw[:, slot, :]).then_inc(dnh_done, 1)

            def gelu_step(s, t, early=False):
                act.wait_ge(gate_done, s + 1)
                if not early:
                    act.wait_ge(h_done, s - 1)
                act.activation(gelu[:, t, :], gate[t][:], ACT.Gelu_apprx_tanh).then_inc(gelu_done, 1)

            def hidden_high(s, slot, t, early=False):
                act.wait_ge(h_done, s + 1)
                if not early:
                    act.wait_ge(down_done, s - 3)
                act.copy(h_high[:, slot, t, :], hidden[:, t, :]).then_inc(hh_done, 1)

            def chunk(c, slot, turn, last=False, early=False, before=None, after=None):
                if before:
                    before(0)
                gelu_step(2 * c, 0, early and c == 0)
                if not last:
                    split_gate_up(1 - slot, c + 1, turn + slot)
                hidden_high(2 * c, slot, 0, early)
                if after:
                    after(0)
                if before:
                    before(1)
                gelu_step(2 * c + 1, 1, early and c == 0)
                split_down(slot, c, turn)
                hidden_high(2 * c + 1, slot, 1, early)
                if after:
                    after(1)

            def x1_high(b, t):
                for k in range(KT):
                    act.wait_ge(x1_done, 1 + k + KT * (t + HALVES * b))
                    act.copy(x_high[:, b, k, t * TN:(t + 1) * TN],
                             x[:, b, k, t * TN:(t + 1) * TN]).then_inc(x1h_done, 1)

            def finish(b):
                for t in range(HALVES):
                    for k in range(KT):
                        n = k + KT * (t + HALVES * b)
                        act.wait_ge(final_mm, n + 1)
                        if b > 0:
                            act.wait_ge(stored, 16 * KT * HALVES * b)
                        act.activation(y[:, k, t * TN:(t + 1) * TN], acc[k][t][:], ACT.Identity,
                                       bias=bias_out[:, b, k:k + 1]).then_inc(final_out, 1)

            split_x_high(0, 0)
            split_gate_up(0, 0, 0)
            split_x_high(0, 1)
            act.wait_ge(neg_done, 1)
            for b in range(BATCHES):
                act.activation(prob[:, b, :], top[:, b, :], ACT.Exp, bias=neg_max[:, b:b + 1]).then_inc(exp_done, 1)
            chunk(0, 0, 0, early=True)
            chunk(1, 1, 0, early=True)
            for t in range(HALVES):
                split_x_high(1, t)
            with act.Fori(1, FOLD_PAIR + 1) as p:
                chunk(2 * p, 0, p)
                chunk(2 * p + 1, 1, p)
            act.wait_ge(fold_out, 3 * BATCHES)
            act.copy(fold_high[:], fold[:]).then_inc(foldh_done, 1)
            with act.Fori(FOLD_PAIR + 1, PAIRS) as p:
                chunk(2 * p, 0, p)
                chunk(2 * p + 1, 1, p)
            for b in range(1, BATCHES):
                p0 = b * PAIRS
                chunk(2 * p0, 0, p0, after=lambda t: x1_high(b - 1, t))
                chunk(2 * p0 + 1, 1, p0)
                finish(b - 1)
                with act.Fori(p0 + 1, p0 + PAIRS - 1) as p:
                    chunk(2 * p, 0, p)
                    chunk(2 * p + 1, 1, p)
            chunk(BATCHES * CHUNKS - 2, 0, BATCHES * PAIRS - 1)
            chunk(BATCHES * CHUNKS - 1, 1, BATCHES * PAIRS - 1, last=True)
            for t in range(HALVES):
                x1_high(BATCHES - 1, t)
            finish(BATCHES - 1)

        @block.vector
        def _(dve):
            steps = 0

            def step(ins):
                nonlocal steps
                steps += 1
                ins.then_inc(route_step, 1)
                dve.wait_ge(route_step, steps)

            def split_x_low(b, t):
                dve.wait_ge(xh_done, 1 + t + HALVES * b)
                dve.tensor_tensor(x_low[:, b, :, t * TN:(t + 1) * TN], x[:, b, :, t * TN:(t + 1) * TN],
                                  x_high[:, b, :, t * TN:(t + 1) * TN].bitcast(F32), ALU.subtract
                                  ).then_inc(xl_done, 1)

            def split_gate_up(slot, c):
                dve.wait_ge(guh_done, c + 1)
                if not isinstance(c, int) or c >= 2:
                    dve.wait_ge(up_done, 2 * c - 2)
                dve.tensor_tensor(gu_low[:, slot, :], gu_raw[:, slot, :], gu_high[:, slot, :].bitcast(F32),
                                  ALU.subtract).then_inc(gul_done, 1)

            def split_down(slot, c):
                dve.wait_ge(dnh_done, c + 1)
                if not isinstance(c, int) or c >= 2:
                    dve.wait_ge(down_done, 2 * c - 2)
                dve.tensor_tensor(dn_low[:, slot, :], dn_raw[:, slot, :], dn_high[:, slot, :].bitcast(F32),
                                  ALU.subtract).then_inc(dnl_done, 1)

            def hidden_step(s, t, p, early=False):
                dve.wait_ge(gelu_done, s + 1)
                dve.wait_ge(up_done, s + 1)
                if not early:
                    dve.wait_ge(hl_done, s - 1)
                dve.scalar_tensor_tensor(hidden[:, t, :], gelu[:, t, :], pair_weight[:, bass.ds(p, 1)],
                                         up[t][:], ALU.mult, ALU.mult).then_inc(h_done, 1)

            def hidden_low(s, slot, t, early=False):
                dve.wait_ge(hh_done, s + 1)
                if not early:
                    dve.wait_ge(down_done, s - 3)
                dve.tensor_tensor(h_low[:, slot, t, :], hidden[:, t, :], h_high[:, slot, t, :].bitcast(F32),
                                  ALU.subtract).then_inc(hl_done, 1)

            def chunk(c, slot, p, last=False, early=False, before=None, after=None):
                if before:
                    before(0)
                hidden_step(2 * c, 0, p, early and c == 0)
                if not last:
                    split_gate_up(1 - slot, c + 1)
                hidden_low(2 * c, slot, 0, early)
                if after:
                    after(0)
                if before:
                    before(1)
                hidden_step(2 * c + 1, 1, p, early and c == 0)
                split_down(slot, c)
                hidden_low(2 * c + 1, slot, 1, early)
                if after:
                    after(1)

            def x1(b, t):
                c = (b + 1) * CHUNKS
                dve.wait_ge(down_done, 2 * c - 1 + t)
                for k in range(KT):
                    dve.tensor_tensor(x[:, b, k, t * TN:(t + 1) * TN], acc[k][t][:],
                                      x[:, b, k, t * TN:(t + 1) * TN], ALU.add).then_inc(x1_done, 1)
                for k in range(KT):
                    dve.wait_ge(x1h_done, 1 + k + KT * (t + HALVES * b))
                    dve.tensor_tensor(x_low[:, b, k, t * TN:(t + 1) * TN], x[:, b, k, t * TN:(t + 1) * TN],
                                      x_high[:, b, k, t * TN:(t + 1) * TN].bitcast(F32), ALU.subtract
                                      ).then_inc(x1l_done, 1)

            split_x_low(0, 0)
            split_gate_up(0, 0)
            split_x_low(0, 1)
            dve.wait_ge(cond_in, 16)
            for b in range(BATCHES):
                dve.max(top[:, b, :], logits[:, b, :]).then_inc(top_done, 1)
            dve.wait_ge(top_done, BATCHES)
            dve.tensor_scalar(neg_max[:], top[:, :, 0], -1.0, None, ALU.mult).then_inc(neg_done, 1)
            for b in range(BATCHES):
                dve.max_index(pick[:, b, :], top[:, b, :], logits[:, b, :]).then_inc(pick_found, 1)
            dve.wait_ge(pick_found, BATCHES)
            dve.tensor_scalar(pick_safe[:], pick[:], float(EXPERTS - 1), None, ALU.min).then_inc(pick_done, 1)
            dve.wait_ge(exp_done, BATCHES)
            step(dve.reduce_sum(prob_sum[:], prob[:], AX.X))
            step(dve.reciprocal(prob_sum[:], prob_sum[:]))
            for b in range(BATCHES):
                step(dve.tensor_scalar(top_w[:, b, :], prob[:, b, 0:TOP_K], prob_sum[:, b:b + 1], None, ALU.mult))
            step(dve.reduce_sum(prob_sum[:], top_w[:], AX.X))
            step(dve.reciprocal(prob_sum[:], prob_sum[:]))
            for b in range(BATCHES):
                step(dve.tensor_scalar(top_w[:, b, :], top_w[:, b, :], prob_sum[:, b:b + 1], None, ALU.mult))
            scale = 1.0 / MOE_LAYERS
            step(dve.tensor_scalar(top_scaled[:], top_w[:], scale, None, ALU.mult))
            step(dve.scalar_tensor_tensor(top_w[:], top_w[:], 1.0 - scale, top_scaled[:], ALU.mult, ALU.add))
            step(dve.memset(pair_weight[:], 1.0))
            for b in range(BATCHES):
                for j in range(TOP_K):
                    a = b * PAIRS + (1 + j) * PPE
                    step(dve.tensor_scalar(pair_weight[:, a:a + PPE], pair_weight[:, a:a + PPE],
                                           top_w[:, b, j:j + 1], None, ALU.mult))

            chunk(0, 0, 0, early=True)
            chunk(1, 1, 0, early=True)
            for t in range(HALVES):
                split_x_low(1, t)
            with dve.Fori(1, FOLD_PAIR) as p:
                chunk(2 * p, 0, p)
                chunk(2 * p + 1, 1, p)

            def fold_stage(n, t):
                dve.wait_ge(fold_mm, n)
                if n == 1:
                    dve.wait_ge(base_done, 1)
                for b, pbank in enumerate((gate[t], up[t])):
                    whole = pbank[:].rearrange("p (k n) -> p k n", k=KT)
                    if n == 1:
                        ins = dve.tensor_tensor(a1[:, b], whole, base[:], ALU.add)
                    elif n == 4:
                        ins = dve.tensor_tensor(bias_out[:, b, :], pbank[:, 0:KT], bias[:, 2, :], ALU.add)
                    else:
                        ins = dve.tensor_copy((r23 if n == 2 else fold)[:, b], whole)
                    ins.then_inc(fold_out, 1)

            chunk(2 * FOLD_PAIR, 0, FOLD_PAIR, before=lambda t: fold_stage(1 + t, t))
            chunk(2 * FOLD_PAIR + 1, 1, FOLD_PAIR, before=lambda t: fold_stage(3 + t, t))
            dve.wait_ge(foldh_done, 1)
            dve.tensor_tensor(fold_low[:], fold[:], fold_high[:].bitcast(F32), ALU.subtract).then_inc(foldl_done, 1)
            with dve.Fori(FOLD_PAIR + 1, PAIRS) as p:
                chunk(2 * p, 0, p)
                chunk(2 * p + 1, 1, p)
            for b in range(1, BATCHES):
                p0 = b * PAIRS
                chunk(2 * p0, 0, p0, after=lambda t: x1(b - 1, t))
                chunk(2 * p0 + 1, 1, p0)
                with dve.Fori(p0 + 1, p0 + PAIRS - 1) as p:
                    chunk(2 * p, 0, p)
                    chunk(2 * p + 1, 1, p)
            chunk(BATCHES * CHUNKS - 2, 0, BATCHES * PAIRS - 1)
            chunk(BATCHES * CHUNKS - 1, 1, BATCHES * PAIRS - 1, last=True)
            for t in range(HALVES):
                x1(BATCHES - 1, t)

        @block.tensor
        def _(pe):
            def three_passes(out, parts, start, stop):
                n = len(parts)
                for i, (w_high, w_low, v_high, v_low) in enumerate(parts):
                    pe.matmul(out, w_high, v_high, start=start and i == 0, stop=False)
                    pe.matmul(out, w_high, v_low, start=False, stop=False)
                    ins = pe.matmul(out, w_low, v_high, start=False, stop=stop and i == n - 1)
                return ins

            def gate_up(c, t, slot, b, early=False):
                s = 2 * c + t
                if t == 0:
                    pe.wait_ge(guh_done, c + 1)
                    pe.wait_ge(gul_done, c + 1)
                if not early:
                    pe.wait_ge(h_done, s - 1)
                for j, (out, done) in enumerate(((gate[t], gate_done), (up[t], up_done))):
                    parts = []
                    for k in range(KT):
                        w = slice((j * KT + k) * P, (j * KT + k + 1) * P)
                        v = slice(t * TN, (t + 1) * TN)
                        parts.append((gu_high[:, slot, w], gu_low[:, slot, w], x_high[:, b, k, v], x_low[:, b, k, v]))
                    three_passes(out[:], parts, True, True).then_inc(done, 1)

            def down(c, t, slot, first=False, last=False):
                s = 2 * c + t
                pe.wait_ge(dnl_done, c + 1)
                pe.wait_ge(hh_done, s + 1)
                pe.wait_ge(hl_done, s + 1)
                for m in range(KT):
                    w = slice(m * P, (m + 1) * P)
                    ins = three_passes(acc[m][t][:], [(dn_high[:, slot, w], dn_low[:, slot, w],
                                                       h_high[:, slot, t, :], h_low[:, slot, t, :])], first, last)
                ins.then_inc(down_done, 1)

            def final(b):
                pe.wait_ge(foldl_done, 1)
                for t in range(HALVES):
                    pe.wait_ge(x1l_done, KT * (t + 1 + HALVES * b))
                    v = slice(t * TN, (t + 1) * TN)
                    for m in range(KT):
                        w = slice(m * P, (m + 1) * P)
                        three_passes(acc[m][t][:], [(fold_high[:, b, k, w], fold_low[:, b, k, w],
                                                     x_high[:, b, k, v], x_low[:, b, k, v]) for k in range(KT)],
                                     True, True).then_inc(final_mm, 1)

            def pair(p, b):
                for slot in range(2):
                    for t in range(HALVES):
                        gate_up(2 * p + slot, t, slot, b)
                        down(2 * p + slot - 1, t, 1 - slot)

            def fold_products(n, s, t):
                pe.wait_ge(h_done, s - 1)
                if n == 1:
                    pe.wait_ge(la_done, BATCHES)
                    pe.wait_ge(small_in, 16 * 6)
                elif n == 2:
                    pe.wait_ge(mixes_done, 2 * BATCHES)
                else:
                    pe.wait_ge(fold_out, 2 * BATCHES)
                for b, out in enumerate((gate[t], up[t])):
                    for m in range(KT):
                        w = slice(m * P, (m + 1) * P)
                        block_out = out[:, m * HID:(m + 1) * HID]
                        if n == 1:
                            ins = pe.matmul(block_out, lb[:, w], la_w[:, b, :], start=True, stop=True)
                            continue
                        if n == 2:
                            parts = [(a2[:, b, k, w], r3[:, b, k, :]) for k in range(KT)]
                        elif n == 3:
                            parts = [(a1[:, b, k, w], r23[:, b, k, :]) for k in range(KT)]
                        else:
                            block_out = out[:, m:m + 1]
                            parts = [(r23[:, b, k, w], bias[:, 0, k:k + 1]) for k in range(KT)]
                            parts += [(r3[:, b, k, w], bias[:, 1, k:k + 1]) for k in range(KT)]
                        for i, (lhsT, rhs) in enumerate(parts):
                            ins = pe.matmul(block_out, lhsT, rhs, start=i == 0, stop=i == len(parts) - 1)
                ins.then_inc(fold_mm, 1)

            for t in range(HALVES):
                pe.wait_ge(xl_done, 1 + t)
                gate_up(0, t, 0, 0, early=True)
            for t in range(HALVES):
                gate_up(1, t, 1, 0)
                down(0, t, 0, first=True)
            with pe.Fori(1, FOLD_PAIR) as p:
                pair(p, 0)
            for n, (slot, t) in enumerate(((0, 0), (0, 1), (1, 0), (1, 1))):
                c = 2 * FOLD_PAIR + slot
                fold_products(n + 1, 2 * c + t, t)
                down(c - 1, t, 1 - slot)
                pe.wait_ge(fold_out, BATCHES * (n + 1))
                gate_up(c, t, slot, 0)
            with pe.Fori(FOLD_PAIR + 1, PAIRS) as p:
                pair(p, 0)
            for b in range(1, BATCHES):
                c = b * CHUNKS
                pe.wait_ge(xl_done, HALVES * (b + 1))
                for t in range(HALVES):
                    gate_up(c, t, 0, b)
                    down(c - 1, t, 1, last=True)
                for t in range(HALVES):
                    gate_up(c + 1, t, 1, b)
                final(b - 1)
                for t in range(HALVES):
                    pe.wait_ge(final_out, KT * (t + 1 + HALVES * (b - 1)))
                    down(c, t, 0, first=True)
                with pe.Fori(b * PAIRS + 1, (b + 1) * PAIRS) as p:
                    pair(p, b)
            for t in range(HALVES):
                down(BATCHES * CHUNKS - 1, t, 1, last=True)
            final(BATCHES - 1)


_OUT = (BATCHES, KT, P, TOKENS)


def kernel(x, cond_8, L0_cond_skill_gate, L0_cond_skill_up, L0_cond_skill_down, L0_cond_shared_gate,
           L0_cond_shared_up, L0_cond_shared_down, L1_cond_W_base, L1_cond_b_base, L1_cond_As, L1_cond_Bs,
           L2_cond_weight, L2_cond_mask, L2_cond_bias, L3_cond_weight, L3_cond_mask, L3_cond_bias):
    import numpy as np
    import concourse.bacc as bacc
    from concourse.bass_utils import run_bass_kernel_spmd

    def experts(skill, shared):
        return np.concatenate([np.asarray(skill), np.asarray(shared)[None]])

    def feature_rows(a):
        return np.swapaxes(a.reshape(*a.shape[:-2], KT, P, a.shape[-1]), -3, -2)

    def chunks(w):
        return feature_rows(w).reshape(EXPERTS + 1, P, KT, CPE, P).transpose(0, 3, 1, 2, 4)

    gates = chunks(experts(L0_cond_skill_gate, L0_cond_shared_gate))
    ups = chunks(experts(L0_cond_skill_up, L0_cond_shared_up))
    gate_up = np.stack([gates, ups], axis=3).reshape(EXPERTS + 1, CPE, P, GU)
    down = experts(L0_cond_skill_down, L0_cond_shared_down).reshape(EXPERTS + 1, CPE, P, HID)
    xT = feature_rows(np.asarray(x).transpose(0, 2, 1)).reshape(BATCHES, P, KT, HALVES, TN).transpose(0, 3, 1, 2, 4)

    def groups_rows(w):
        return feature_rows(np.asarray(w)).transpose(1, 0, 2, 3).reshape(P, GROUPS, KT * HID)

    arrays = {
        "xT": xT,
        "cond": np.asarray(cond_8),
        "w_gate_up": gate_up,
        "w_down": down,
        "w_base": feature_rows(np.asarray(L1_cond_W_base)),
        "lora_a": np.asarray(L1_cond_As).reshape(EXPERTS * RANK, HID),
        "lora_b": np.asarray(L1_cond_Bs).transpose(0, 2, 1).reshape(EXPERTS * RANK, HID),
        "mix2": groups_rows(L2_cond_weight),
        "mask2": feature_rows(np.asarray(L2_cond_mask)),
        "mix3": groups_rows(np.asarray(L3_cond_weight).transpose(0, 2, 1)),
        "mask3": feature_rows(np.asarray(L3_cond_mask).T),
        "biases": np.stack([np.asarray(v).reshape(KT, P) for v in (L1_cond_b_base, L2_cond_bias, L3_cond_bias)]
                           ).transpose(2, 0, 1),
    }
    nc = bacc.Bacc("TRN2", target_bir_lowering=False, num_devices=1)
    sent, args = {}, []
    for name, a in arrays.items():
        sent[name] = np.ascontiguousarray(a)
        args.append(nc.dram_tensor(name, a.shape, mybir.dt.from_np(a.dtype), kind="ExternalInput").ap())
    args.append(nc.dram_tensor("outT", _OUT, F32, kind="ExternalOutput").ap())
    bass_moe_lora_masked_mixtures(nc, *args)
    got = run_bass_kernel_spmd(nc, [sent], core_ids=[0]).results[0]["outT"]
    return got.reshape(BATCHES, HID, TOKENS).transpose(0, 2, 1)
```
